# Optimizing a Trainium2 kernel written in Bass

```python
import numpy as np
import jax
import jax.numpy as jnp

def _softmax(x, axis=-1):
    return jax.nn.softmax(x, axis=axis)
def _gelu(x):
    return jax.nn.gelu(x, approximate=True)
def _silu(x):
    return jax.nn.silu(x)
def _sigmoid(x):
    return jax.nn.sigmoid(x)
def _layernorm(x, axis=-1, eps=1e-5):
    m = jnp.mean(x, axis=axis, keepdims=True)
    v = jnp.var(x, axis=axis, keepdims=True)
    return (x - m) / jnp.sqrt(v + eps)
def _scatter_add(tgt, idx, src, axis=0):
    return tgt.at[idx].add(src)
def _segment_sum(src, seg, n):
    return jax.ops.segment_sum(src, seg, n)

kernel_name = 'mk_adj_ffn_d2_adj_256_b7472e'

def setup_inputs(seed: int = 0):
    np.random.seed(seed)
    _w = jnp.asarray
    def _rec_inputs():
        import jax
        import jax.numpy as jnp
        _gk = jax.random.key(seed)
        x = -0.0002928 + 1 * jax.random.normal(jax.random.fold_in(_gk, 1), (64, 256, 256), jnp.float32)
        _a = jax.random.bernoulli(jax.random.fold_in(_gk, 2), 0.0625, (64, 256, 256))
        adj = _a.astype(jnp.int32)
        return x, adj
    x, adj = _rec_inputs()
    def _L0_gnn_setup():
        import jax, jax.numpy as jnp
        import numpy as np
        NEG_BIG = -9000000000000000.0
        ALPHA = 0.2
        key = jax.random.key(seed)
        k1, k2, k3, k4 = jax.random.split(key, 4)
        B, N, Fin, Fout = (8, 2048, 256, 256)
        h = jax.random.normal(k1, (B, N, Fin), dtype=jnp.float32)
        adj = jax.random.randint(k2, (B, N, N), 0, 2, dtype=jnp.int32)
        limW = 1.414 * np.sqrt(6.0 / (Fin + Fout))
        W = jax.random.uniform(k3, (Fin, Fout), jnp.float32, -limW, limW)
        lima = 1.414 * np.sqrt(6.0 / (2 * Fout + 1))
        a = jax.random.uniform(k4, (2 * Fout, 1), jnp.float32, -lima, lima)
        return {'h': h, 'adj': adj, 'W': W, 'a': a}
    _L0_gnn_all = _L0_gnn_setup()
    _L0_gnn_in = {k: v for k, v in _L0_gnn_all.items() if k in ('W', 'a', )}
    del _L0_gnn_all

    def _L0_ffn_setup():
        import jax, jax.numpy as jnp
        import numpy as np
        D_MODEL = 256
        D_STATE = 64
        D_CONV = 4
        EXPAND = 2
        HEADDIM = 64
        D_INNER = EXPAND * D_MODEL
        NHEADS = D_INNER // HEADDIM
        CONV_DIM = D_INNER + 2 * D_STATE
        D_IN_PROJ = 2 * D_INNER + 2 * D_STATE + NHEADS
        CHUNK = 256
        EPS = 1e-05

        def segsum(a):
            T = a.shape[-1]
            cs = jnp.cumsum(a, axis=-1)
            ss = cs[..., :, None] - cs[..., None, :]
            mask = jnp.tril(jnp.ones((T, T), dtype=bool))
            return jnp.where(mask, ss, -jnp.inf)

        def mamba2_block(x, W_in, conv_w, conv_b, dt_bias, A_log, D, norm_w, W_out, W_lin, b_lin):
            Bsz, L, _ = x.shape
            zxbcdt = x @ W_in
            z, xBC, dt = jnp.split(zxbcdt, [D_INNER, D_INNER + CONV_DIM], axis=-1)
            xp = jnp.pad(xBC, ((0, 0), (D_CONV - 1, 0), (0, 0)))
            conv = conv_b + sum((xp[:, k:k + L, :] * conv_w[:, k] for k in range(D_CONV)))
            xBC = jax.nn.silu(conv)
            xh, Bmat, Cmat = jnp.split(xBC, [D_INNER, D_INNER + D_STATE], axis=-1)
            dt = jax.nn.softplus(dt + dt_bias)
            A = -jnp.exp(A_log)
            nc = L // CHUNK
            xh = xh.reshape(Bsz, nc, CHUNK, NHEADS, HEADDIM)
            Bc = Bmat.reshape(Bsz, nc, CHUNK, D_STATE)
            Cc = Cmat.reshape(Bsz, nc, CHUNK, D_STATE)
            dtc = dt.reshape(Bsz, nc, CHUNK, NHEADS)
            dA = jnp.einsum('bclh,h->bhcl', dtc, A)
            A_cum = jnp.cumsum(dA, axis=-1)
            Lmat = jnp.exp(segsum(dA))
            xdt = xh * dtc[..., None]
            Y_diag = jnp.einsum('bcln,bcsn,bhcls,bcshp->bclhp', Cc, Bc, Lmat, xdt)
            decay_states = jnp.exp(A_cum[..., -1:] - A_cum)
            states = jnp.einsum('bcln,bhcl,bclhp->bchpn', Bc, decay_states, xdt)
            chunk_decay = jnp.exp(A_cum[..., -1])

            def step(h, inp):
                s, d = inp
                return (h * d[..., None, None] + s, h)
            _, prevs = jax.lax.scan(step, jnp.zeros_like(states[:, 0]), (jnp.moveaxis(states, 1, 0), jnp.moveaxis(chunk_decay, 2, 0)))
            prevs = jnp.moveaxis(prevs, 0, 1)
            Y_off = jnp.einsum('bcln,bchpn,bhcl->bclhp', Cc, prevs, jnp.exp(A_cum))
            Y = (Y_diag + Y_off + xh * D[:, None]).reshape(Bsz, L, D_INNER)
            Y = Y * jax.nn.silu(z)
            Y = Y * jax.lax.rsqrt(jnp.mean(Y * Y, axis=-1, keepdims=True) + EPS) * norm_w
            out = Y @ W_out
            return out @ W_lin + b_lin
        key = jax.random.key(seed)
        ks = jax.random.split(key, 12)
        B, L = (8, 4096)

        def gauss(k, shape, scale):
            return jax.random.normal(k, shape, dtype=jnp.float32) * scale
        return {'x': gauss(ks[0], (B, L, D_MODEL), 1.0), 'W_in': gauss(ks[1], (D_MODEL, D_IN_PROJ), D_MODEL ** (-0.5)), 'conv_w': gauss(ks[2], (CONV_DIM, D_CONV), 0.3), 'conv_b': gauss(ks[3], (CONV_DIM,), 0.1), 'dt_bias': jax.random.uniform(ks[4], (NHEADS,), minval=-4.0, maxval=-1.0), 'A_log': jnp.log(jax.random.uniform(ks[5], (NHEADS,), minval=1.0, maxval=16.0)), 'D': jnp.ones((NHEADS,), jnp.float32), 'norm_w': jnp.ones((D_INNER,), jnp.float32), 'W_out': gauss(ks[6], (D_INNER, D_MODEL), D_INNER ** (-0.5)), 'W_lin': gauss(ks[7], (D_MODEL, D_MODEL), D_MODEL ** (-0.5)), 'b_lin': jnp.zeros((D_MODEL,), jnp.float32)}
    _L0_ffn_all = _L0_ffn_setup()
    _L0_ffn_in = {k: v for k, v in _L0_ffn_all.items() if k in ('W_in', 'conv_w', 'conv_b', 'dt_bias', 'A_log', 'D', 'norm_w', 'W_out', 'W_lin', 'b_lin', )}
    del _L0_ffn_all

    def _L1_gnn_setup():
        import jax, jax.numpy as jnp
        import numpy as np
        B, N, D_IN, D_OUT, R = (8, 2048, 256, 256, 4)
        key = jax.random.key(seed)
        k1, k2, k3, k4 = jax.random.split(key, 4)
        x = jax.random.normal(k1, (B, N, D_IN), dtype=jnp.float32)
        adj = jnp.zeros((1,), dtype=jnp.float32)
        relation = jax.random.randint(k2, (B, N, N), 0, R + 1, dtype=jnp.int32)
        weight = jax.random.normal(k3, (R, D_IN, D_OUT), dtype=jnp.float32) * 0.05
        bias = jax.random.normal(k4, (D_OUT,), dtype=jnp.float32) * 0.05
        return {'x': x, 'adj': adj, 'relation': relation, 'weight': weight, 'bias': bias}
    _L1_gnn_all = _L1_gnn_setup()
    _L1_gnn_in = {k: v for k, v in _L1_gnn_all.items() if k in ('adj', 'weight', 'bias', )}
    del _L1_gnn_all

    def _L1_ffn_setup():
        import math
        import jax, jax.numpy as jnp
        import numpy as np
        CAPACITY_FACTOR = 1.25
        key = jax.random.key(seed)
        ks = jax.random.split(key, 5)
        B, L, D, F, E = (8, 8192, 256, 1024, 8)
        h = jax.random.normal(ks[0], (B, L, D), dtype=jnp.float32)
        gate_w = jax.random.normal(ks[1], (D, E), dtype=jnp.float32) * 0.02
        gate_b = jnp.zeros((E,), dtype=jnp.float32)
        w1 = jax.random.normal(ks[2], (E, D, F), dtype=jnp.float32) * (1.0 / math.sqrt(D))
        b1 = jnp.zeros((E, F), dtype=jnp.float32)
        w2 = jax.random.normal(ks[3], (E, F, D), dtype=jnp.float32) * (1.0 / math.sqrt(F))
        b2 = jnp.zeros((E, D), dtype=jnp.float32)
        return {'h': h, 'gate_w': gate_w, 'gate_b': gate_b, 'w1': w1, 'b1': b1, 'w2': w2, 'b2': b2}
    _L1_ffn_all = _L1_ffn_setup()
    _L1_ffn_in = {k: v for k, v in _L1_ffn_all.items() if k in ('gate_w', 'gate_b', 'w1', 'b1', 'w2', 'b2', )}
    del _L1_ffn_all

    return {
        "x": x,
        "adj": adj,
        "L0_gnn_W": _L0_gnn_in["W"],
        "L0_gnn_a": _L0_gnn_in["a"],
        "L0_ffn_W_in": _L0_ffn_in["W_in"],
        "L0_ffn_conv_w": _L0_ffn_in["conv_w"],
        "L0_ffn_conv_b": _L0_ffn_in["conv_b"],
        "L0_ffn_dt_bias": _L0_ffn_in["dt_bias"],
        "L0_ffn_A_log": _L0_ffn_in["A_log"],
        "L0_ffn_D": _L0_ffn_in["D"],
        "L0_ffn_norm_w": _L0_ffn_in["norm_w"],
        "L0_ffn_W_out": _L0_ffn_in["W_out"],
        "L0_ffn_W_lin": _L0_ffn_in["W_lin"],
        "L0_ffn_b_lin": _L0_ffn_in["b_lin"],
        "L1_gnn_adj": _L1_gnn_in["adj"],
        "L1_gnn_weight": _L1_gnn_in["weight"],
        "L1_gnn_bias": _L1_gnn_in["bias"],
        "L1_ffn_gate_w": _L1_ffn_in["gate_w"],
        "L1_ffn_gate_b": _L1_ffn_in["gate_b"],
        "L1_ffn_w1": _L1_ffn_in["w1"],
        "L1_ffn_b1": _L1_ffn_in["b1"],
        "L1_ffn_w2": _L1_ffn_in["w2"],
        "L1_ffn_b2": _L1_ffn_in["b2"],
    }

def reference(x, adj, L0_gnn_W, L0_gnn_a, L0_ffn_W_in, L0_ffn_conv_w, L0_ffn_conv_b, L0_ffn_dt_bias, L0_ffn_A_log, L0_ffn_D, L0_ffn_norm_w, L0_ffn_W_out, L0_ffn_W_lin, L0_ffn_b_lin, L1_gnn_adj, L1_gnn_weight, L1_gnn_bias, L1_ffn_gate_w, L1_ffn_gate_b, L1_ffn_w1, L1_ffn_b1, L1_ffn_w2, L1_ffn_b2):
    import jax
    import jax.numpy as jnp
    def _L0_gnn_ref(h, adj, W, a):
        import jax, jax.numpy as jnp
        import numpy as np
        NEG_BIG = -9000000000000000.0
        ALPHA = 0.2
        Fout = W.shape[1]
        wh = jnp.einsum('bni,io->bno', h, W)
        a1 = a[:Fout, 0]
        a2 = a[Fout:, 0]
        s1 = wh @ a1
        s2 = wh @ a2
        e = jax.nn.leaky_relu(s1[:, :, None] + s2[:, None, :], negative_slope=ALPHA)
        e = jnp.where(adj > 0, e, NEG_BIG)
        attention = jax.nn.softmax(e, axis=2)
        h_prime = jnp.einsum('bmn,bno->bmo', attention, wh)
        return h_prime

    def _L0_ffn_ref(x, W_in, conv_w, conv_b, dt_bias, A_log, D, norm_w, W_out, W_lin, b_lin):
        import jax, jax.numpy as jnp
        import numpy as np
        D_MODEL = 256
        D_STATE = 64
        D_CONV = 4
        EXPAND = 2
        HEADDIM = 64
        D_INNER = EXPAND * D_MODEL
        NHEADS = D_INNER // HEADDIM
        CONV_DIM = D_INNER + 2 * D_STATE
        D_IN_PROJ = 2 * D_INNER + 2 * D_STATE + NHEADS
        CHUNK = 256
        EPS = 1e-05

        def segsum(a):
            T = a.shape[-1]
            cs = jnp.cumsum(a, axis=-1)
            ss = cs[..., :, None] - cs[..., None, :]
            mask = jnp.tril(jnp.ones((T, T), dtype=bool))
            return jnp.where(mask, ss, -jnp.inf)

        def mamba2_block(x, W_in, conv_w, conv_b, dt_bias, A_log, D, norm_w, W_out, W_lin, b_lin):
            Bsz, L, _ = x.shape
            zxbcdt = x @ W_in
            z, xBC, dt = jnp.split(zxbcdt, [D_INNER, D_INNER + CONV_DIM], axis=-1)
            xp = jnp.pad(xBC, ((0, 0), (D_CONV - 1, 0), (0, 0)))
            conv = conv_b + sum((xp[:, k:k + L, :] * conv_w[:, k] for k in range(D_CONV)))
            xBC = jax.nn.silu(conv)
            xh, Bmat, Cmat = jnp.split(xBC, [D_INNER, D_INNER + D_STATE], axis=-1)
            dt = jax.nn.softplus(dt + dt_bias)
            A = -jnp.exp(A_log)
            nc = L // CHUNK
            xh = xh.reshape(Bsz, nc, CHUNK, NHEADS, HEADDIM)
            Bc = Bmat.reshape(Bsz, nc, CHUNK, D_STATE)
            Cc = Cmat.reshape(Bsz, nc, CHUNK, D_STATE)
            dtc = dt.reshape(Bsz, nc, CHUNK, NHEADS)
            dA = jnp.einsum('bclh,h->bhcl', dtc, A)
            A_cum = jnp.cumsum(dA, axis=-1)
            Lmat = jnp.exp(segsum(dA))
            xdt = xh * dtc[..., None]
            Y_diag = jnp.einsum('bcln,bcsn,bhcls,bcshp->bclhp', Cc, Bc, Lmat, xdt)
            decay_states = jnp.exp(A_cum[..., -1:] - A_cum)
            states = jnp.einsum('bcln,bhcl,bclhp->bchpn', Bc, decay_states, xdt)
            chunk_decay = jnp.exp(A_cum[..., -1])

            def step(h, inp):
                s, d = inp
                return (h * d[..., None, None] + s, h)
            _, prevs = jax.lax.scan(step, jnp.zeros_like(states[:, 0]), (jnp.moveaxis(states, 1, 0), jnp.moveaxis(chunk_decay, 2, 0)))
            prevs = jnp.moveaxis(prevs, 0, 1)
            Y_off = jnp.einsum('bcln,bchpn,bhcl->bclhp', Cc, prevs, jnp.exp(A_cum))
            Y = (Y_diag + Y_off + xh * D[:, None]).reshape(Bsz, L, D_INNER)
            Y = Y * jax.nn.silu(z)
            Y = Y * jax.lax.rsqrt(jnp.mean(Y * Y, axis=-1, keepdims=True) + EPS) * norm_w
            out = Y @ W_out
            return out @ W_lin + b_lin
        return mamba2_block(x, W_in, conv_w, conv_b, dt_bias, A_log, D, norm_w, W_out, W_lin, b_lin)

    def _L1_gnn_ref(x, adj, relation, weight, bias):
        import jax, jax.numpy as jnp
        import numpy as np
        B, N, D_IN, D_OUT, R = (8, 2048, 256, 256, 4)
        rel_ids = jnp.arange(1, weight.shape[0] + 1, dtype=relation.dtype)
        masks = (relation[None] == rel_ids[:, None, None, None]).astype(x.dtype)
        h = jnp.einsum('rbnm,bmd->rbnd', masks, x)
        y = jnp.einsum('rbnd,rdo->bno', h, weight)
        return y + bias

    def _L1_ffn_ref(h, gate_w, gate_b, w1, b1, w2, b2):
        import math
        import jax, jax.numpy as jnp
        import numpy as np
        CAPACITY_FACTOR = 1.25
        B, L, D = h.shape
        E = gate_w.shape[1]
        T = B * L
        C = max(1, math.ceil(CAPACITY_FACTOR * T / E))
        x = h.reshape(T, D)
        logits = x @ gate_w + gate_b
        probs = jax.nn.softmax(logits, axis=-1)
        idx = jnp.argmax(probs, axis=-1)
        prb = jnp.take_along_axis(probs, idx[:, None], axis=1)[:, 0]
        one_hot = jax.nn.one_hot(idx, E, dtype=jnp.float32)
        pos = (jnp.cumsum(one_hot, axis=0) * one_hot).sum(-1).astype(jnp.int32) - 1
        kept = pos < C
        pos_safe = jnp.where(kept, pos, C)
        buf = jnp.zeros((E, C, D), dtype=h.dtype).at[idx, pos_safe].set(x, mode='drop')
        hmid = jax.nn.relu(jnp.einsum('ecd,edf->ecf', buf, w1) + b1[:, None, :])
        ybuf = jnp.einsum('ecf,efd->ecd', hmid, w2) + b2[:, None, :]
        pos_g = jnp.minimum(pos, C - 1)
        y_tok = ybuf[idx, pos_g] * (prb * kept)[:, None]
        y = y_tok.reshape(B, L, D)
        y = jnp.nan_to_num(y, nan=0.0, posinf=10000.0, neginf=-10000.0)
        return y

    x = x + _L0_gnn_ref(_layernorm(x, axis=-1), adj, L0_gnn_W, L0_gnn_a)
    x = x + _L0_ffn_ref(_layernorm(x, axis=-1), L0_ffn_W_in, L0_ffn_conv_w, L0_ffn_conv_b, L0_ffn_dt_bias, L0_ffn_A_log, L0_ffn_D, L0_ffn_norm_w, L0_ffn_W_out, L0_ffn_W_lin, L0_ffn_b_lin)
    x = x + _L1_gnn_ref(_layernorm(x, axis=-1), L1_gnn_adj, adj, L1_gnn_weight, L1_gnn_bias)
    x = x + _L1_ffn_ref(_layernorm(x, axis=-1), L1_ffn_gate_w, L1_ffn_gate_b, L1_ffn_w1, L1_ffn_b1, L1_ffn_w2, L1_ffn_b2)
    return x


_drawn_inputs = setup_inputs


def setup_inputs(seed=0):
    import zlib

    import numpy as np

    out = dict(_drawn_inputs(seed))
    spreads = {'L0_ffn_D': (1.0, 0.2),
     'L0_ffn_norm_w': (1.0, 0.2),
     'L0_ffn_b_lin': (0.0, 0.1),
     'L1_ffn_gate_b': (0.0, 0.48),
     'L1_ffn_b1': (0.0, 2.0),
     'L1_ffn_b2': (0.0, 0.8)}
    factors = {'L1_gnn_bias': 5.152}
    for name, (base, spread) in spreads.items():
        noise = np.random.default_rng([zlib.crc32(name.encode()), seed]).standard_normal(out[name].shape)
        drawn = base * np.exp(spread * noise) if base else spread * noise
        out[name] = jnp.asarray(drawn.astype(out[name].dtype))
    for name, factor in factors.items():
        out[name] = (out[name] * factor).astype(out[name].dtype)
    return out
```

```python
from contextlib import ExitStack

import concourse.bass as bass
from concourse import mybir

ALU = mybir.AluOpType
ACT = mybir.ActivationFunctionType
F32 = mybir.dt.float32
BF16 = mybir.dt.bfloat16
I32 = mybir.dt.int32
AX = mybir.AxisListType

P = 128
EPS = 1e-5
NEG_BIG = -9000000000000000.0
NEG_MASK = -1e30
SLOPE = 0.2


def need(eng, sem, n):
    if isinstance(n, int) and n <= 0:
        return
    eng.wait_ge(sem, n)


class Chain:

    def __init__(self, sem, per):
        self.sem, self.per, self.n = sem, per, 0

    def start(self):
        self.n = 0

    def link(self, eng, ins, b, carrier=None):
        self.n += 1
        assert self.n <= self.per
        ins.then_inc(self.sem, 1)
        eng.wait_ge(self.sem, b * self.per + self.n)
        if carrier:
            carrier(eng)

    def end(self):
        assert self.n == self.per, self.n


def graph_mamba_moe(nc, io, out):
    x_d, adj_d, adjt_d = io["x"], io["adj"], io["adjT"]
    NB, N, D = x_d.shape
    T = N // P
    DK = D // P
    DIN = io["L0_ffn_W_out"].shape[0]
    H = io["L0_ffn_D"].shape[0]
    HD = DIN // H
    XB = DIN // P
    CONVC = io["L0_ffn_conv_w"].shape[0]
    TAPS = io["L0_ffn_conv_w"].shape[1]
    NS = (CONVC - DIN) // 2
    CB = CONVC // P
    R = io["L1_gnn_weight"].shape[0]
    E = io["L1_ffn_gate_w"].shape[1]
    FF = io["L1_ffn_w1"].shape[2]
    FB = FF // P
    NT = NB * N
    CAP = -(-5 * NT // (4 * E))
    SLOTS = E * CAP
    TG = 4
    GROUP = TG * P
    EG = CAP // GROUP
    SC = CAP // P
    ROW = D + 4
    assert T == 2 and DK == 2 and XB == 4 and CB == XB + 1 and H == 2 * XB and 2 * NS == P
    assert R == 4 and E == 8 and CAP % GROUP == 0 and EG * TG == SC and NB >= 4
    EXPO = (2, 5, 3, 4)
    TRI = N + P

    ctx = ExitStack()
    with ctx:
        ctx.enter_context(nc.allow_non_contiguous_dma(reason="a few small vectors, one value to a partition"))

        def sb(name, shape, dt=F32):
            return ctx.enter_context(nc.sbuf_tensor(name, shape, dt))

        def sem(name):
            return ctx.enter_context(nc.semaphore(name))

        bank = [ctx.enter_context(nc.psum_tensor(f"bank{i}", [P, 512], F32)) for i in range(8)]
        rows_d = nc.dram_tensor("token_rows", [NT, ROW], F32, kind="Internal").ap()
        ids_d = nc.dram_tensor("slot_ids", [SLOTS + NT, 1], I32, kind="Internal").ap()

        identf = sb("identf", [P, P])
        identb = sb("identb", [P, P], BF16)
        onesb = sb("onesb", [P, P], BF16)
        triub = sb("triub", [P, P], BF16)
        negmask = sb("negmask", [P, P], BF16)
        sel = sb("sel", [72, H, P], BF16)
        selneg = sb("selneg", [72, H, N], BF16)
        ones_row = sb("ones_row", [P, N])
        mhalf = sb("mhalf", [P, T])
        BEATS = 256
        beats = sb("beats", [P, BEATS])
        w_gat = sb("w_gat", [P, DK, D])
        a_bc = sb("a_bc", [P, 2, D])
        wa = sb("wa", [P, 2, DK])
        wa2 = sb("wa2", [P, DK, P])
        w_in = sb("w_in", [P, DK, 2 * DIN + 2 * NS + H])
        conv_w = sb("conv_w", [P, CB, TAPS])
        conv_b = sb("conv_b", [P, CB])
        dt_b = sb("dt_b", [H, 1])
        a_log = sb("a_log", [H, 1])
        a_neg = sb("a_neg", [H, 2])
        d_col = sb("d_col", [P, XB])
        norm_w = sb("norm_w", [P, XB])
        w_lin = sb("w_lin", [P, DK, D])
        w_proj = sb("w_proj", [P, XB, D])
        b_lin = sb("b_lin", [P, D])
        w_rel = sb("w_rel", [P, R, DK, D])
        b_rel = sb("b_rel", [P, D])
        gate_w = sb("gate_w", [P, DK, E])
        gate_b = sb("gate_b", [P, T, E])
        rev = sb("rev", [P, T, E])
        lim = sb("lim", [P, T, E])
        base = sb("base", [P, E])
        tokf = sb("tokf", [P, T])
        ids_init = sb("ids_init", [P, SLOTS // P], I32)

        def pair(name, dt=F32, n=D):
            return sb(name, [P, 2, n], dt)

        x = pair("x_sb")
        adj = pair("adj_sb", I32, N)
        adjt = pair("adjt_sb", I32, N)
        noedge = pair("noedge", F32, N)
        xn0, xn0T, wh = pair("xn0"), pair("xn0T", F32, N), pair("wh")
        z, e, prob, probT = pair("z", F32, N), pair("e", F32, N), pair("prob", F32, N), pair("probT", F32, N)
        s1 = sb("s1", [P, T])
        emax, nmax, esum, rsum = sb("emax", [P, T]), sb("nmax", [P, T]), sb("esum", [P, T]), sb("rsum", [P, T])
        x1, xn1, xn1T = pair("x1"), pair("xn1"), pair("xn1T", F32, N)
        stats = [sb(f"stats{i}", [P, T, 6]) for i in range(4)]
        mv = [sb(f"mv{i}", [P, T, 2]) for i in range(4)]
        ve = [sb(f"ve{i}", [P, T]) for i in range(5)]
        rstd = [sb(f"rstd{i}", [P, T]) for i in range(5)]

        x1b = pair("x1b")
        conv = sb("conv", [P, CB, N])
        xs = sb("xs", [P, XB, N])
        zs = sb("zs", [P, XB, N])
        bT, cT = sb("bT", [NS, N]), sb("cT", [NS, N])
        dt_abs, dt_exp, dt_ln = sb("dt_abs", [H, N]), sb("dt_exp", [H, N]), sb("dt_ln", [H, N])
        dt_pos, dt, dA, cs = sb("dt_pos", [H, N]), sb("dt", [H, N]), sb("dA", [H, N]), sb("cs", [H, N])
        cs3 = sb("cs3", [72, N], BF16)
        cs_r, cs_m = sb("cs_r", [H, N]), sb("cs_m", [H, N], BF16)
        xdt = pair("xdt", F32, DIN)
        g = sb("g", [P, TRI + T * H])
        dtT = g[:, TRI:TRI + T * H].rearrange("p (t h) -> p t h", t=T)
        decay = sb("decay", [P, H, TRI])
        junk = decay[:, :, :].rearrange("p h n -> p (h n)")[:, 0:2 * DK * D].rearrange(
            "p (i k d) -> p i k d", i=2, k=DK)
        y, y2 = sb("y", [P, XB, N]), sb("y2", [P, XB, N])
        x2, x2b = pair("x2"), pair("x2b")

        xn2 = pair("xn2")
        xp = [pair(f"xp{i}", BF16) for i in range(3)]
        xr, xm = pair("xr"), pair("xm")
        masks = sb("masks", [P, T, R, N], BF16)
        hT = sb("hT", [P, DK, R * N])
        w_out = hT[:, 0, :].rearrange("p (c d) -> p c d", c=XB)
        w_outT = hT[:, 1, :].rearrange("p (k c) -> p k c", k=DK)
        row = sb("row", [P, T, ROW])
        xn3, xn3T = pair("xn3"), pair("xn3T", F32, N)
        lg, lg2, ge, eq, rv = (sb(n_, [P, T, E]) for n_ in ("lg", "lg2", "ge", "eq", "rv"))
        oh = sb("oh", [P, T, E])
        ohb = sb("ohb", [P, T, E], BF16)
        cum, cumo, limo = (sb(n_, [P, T, E]) for n_ in ("cum", "cumo", "limo"))
        lmax, gsum, grec, gmax, rmax, prb, slot1, lm, kept, tr1, df, kd = (
            sb(n_, [P, T]) for n_ in
            ("lmax", "gsum", "grec", "gmax", "rmax", "prb", "slot1", "lm", "kept", "tr1", "df", "kd"))
        slot = sb("slot", [P, T], I32)
        tid = sb("tid", [P, T], I32)

        w1 = [sb(f"w1_{i}", [P, DK, FF]) for i in range(2)]
        w2 = [sb(f"w2_{i}", [P, FB, D]) for i in range(2)]
        b1 = [sb(f"b1_{i}", [P, FB]) for i in range(2)]
        b2 = [sb(f"b2_{i}", [P, D]) for i in range(2)]
        ids = [sb(f"ids_{i}", [P, SC], I32) for i in range(2)]
        idc = [sb(f"idc_{i}", [P, SC], I32) for i in range(2)]
        xg = [sb(f"xg_{i}", [P, TG, ROW]) for i in range(2)]
        xgn = xdt[:, :, :].rearrange("p t (a d) -> p (t a) d", d=D)
        xgT = zs[:, :, :].rearrange("p (k a) n -> p k (a n)", k=DK)
        yo = [hT[:, i, :].rearrange("p (j d) -> p j d", d=D) for i in range(2)]
        hid_lo = decay[:, :, :].rearrange("p h n -> p (h n)").rearrange("p (f n) -> p f n", n=GROUP)
        hid_hi = y[:, :, :].rearrange("p a n -> p (a n)").rearrange("p (f n) -> p f n", n=GROUP)
        LO = H * TRI // GROUP

        def hid(f):
            return hid_lo[:, f, :] if f < LO else hid_hi[:, f - LO, :]

        marks = masks[:, :, :, :].rearrange("p t r n -> p (t r n)").bitcast(mybir.dt.uint8)
        isp, isn, isnan = (marks[:, i * TG * D:(i + 1) * TG * D].rearrange("p (j d) -> p j d", d=D) for i in range(3))
        cpos, cneg, czero = sb("cpos", [P, D]), sb("cneg", [P, D]), sb("czero", [P, D])

        loads, built, built_v, prep_pe, prep_v, prep_a = map(
            sem, ("loads", "built", "built_v", "prep_pe", "prep_v", "prep_a"))
        x_in, adj_in, adjt_in = map(sem, ("x_in", "adj_in", "adjt_in"))
        var_ready = [sem(f"var_ready{i}") for i in range(5)]
        rstd_ready = [sem(f"rstd_ready{i}") for i in range(5)]
        ch1, ch1b, ch2, ch3, chr_ = (Chain(sem(n_), k_) for n_, k_ in
                                     (("dve_gat", 5), ("dve_gat_norm", 2), ("dve_mamba", 5), ("dve_rel", 2),
                                      ("dve_route", 15)))
        noedge_ready, xn0_ready, xn0_turned, xn0T_ready, wh_made, wh_ready, s_made, z_ready = map(
            sem, ("noedge_ready", "xn0_ready", "xn0_turned", "xn0T_ready", "wh_made", "wh_ready", "s_made", "z_ready"))
        s1_ready, e_ready, prob_ready, prob_turned, probT_ready, hp_made, x1_ready, xn1_ready, xn1_turned, xn1T_ready = map(
            sem, ("s1_ready", "e_ready", "prob_ready", "prob_turned", "probT_ready", "hp_made", "x1_ready", "xn1_ready",
                  "xn1_turned", "xn1T_ready"))
        x1b_ready, proj_made, tap_ready, conv_ready, dt_act, dt_ready, cs_ready, zs_ready, bc_ready, xs_ready = map(
            sem, ("x1b_ready", "proj_made", "tap_ready", "conv_ready", "dt_act", "dt_ready", "cs_ready", "zs_ready",
                  "bc_ready", "xs_ready"))
        g_made, g_ready, x_turned, xdt_ready, expo_made, decay_ready, m_ready, y_made = map(
            sem, ("g_made", "g_ready", "x_turned", "xdt_ready", "expo_made", "decay_ready",
                  "m_ready", "y_made"))
        yd_ready, yz_ready, y2_ready, out_made, x2_ready, ms_ready = map(
            sem, ("yd_ready", "yz_ready", "y2_ready", "out_made", "x2_ready", "ms_ready"))
        x2b_ready, masks_ready, xn2_ready, part_a, part_v, h_made, hT_ready, gy_made, x3_ready = map(
            sem, ("x2b_ready", "masks_ready", "xn2_ready", "part_a", "part_v", "h_made", "hT_ready",
                  "gy_made", "x3_ready"))
        xn3_ready, xn3_turned, xn3T_ready, gate_made, lg_ready, ge_ready, oh_ready, cum_made, base_ready = map(
            sem, ("xn3_ready", "xn3_turned", "xn3T_ready", "gate_made", "lg_ready", "ge_ready", "oh_ready", "cum_made",
                  "base_ready"))
        row_ready, slot_ready, rows_out, x3_out, ids_set, ids_out = map(
            sem, ("row_ready", "slot_ready", "rows_out", "x3_out", "ids_set", "ids_out"))
        ew_in = [sem(f"ew_in{i}") for i in range(2)]
        eid_in = [sem(f"eid_in{i}") for i in range(2)]
        gath = [sem(f"gath{i}") for i in range(2)]
        put = [sem(f"put{i}") for i in range(2)]
        idc_ready, xgn_ready, xg_turned, xgT_ready, up_made, hid_act, hid_dve, down_made, sum_ready, yo_ready = map(
            sem, ("idc_ready", "xgn_ready", "xg_turned", "xgT_ready", "up_made", "hid_act", "hid_dve", "down_made",
                  "sum_ready", "yo_ready"))
        che = Chain(sem("dve_expert"), 5)
        carried = sem("carried")
        expert_done = [sem(f"expert_done{i}") for i in range(2)]

        def by_tile(a):
            return a.rearrange("(t p) d -> p t d", p=P)

        def col(a):
            return a.rearrange("(h o) -> h o", o=1)

        small = [
            (w_gat, by_tile(io["L0_gnn_W"])),
            (a_bc, io["L0_gnn_a"].rearrange("(a d) o -> (a o) d", a=2).partition_broadcast(P)),
            (w_in, by_tile(io["L0_ffn_W_in"])),
            (conv_w, by_tile(io["L0_ffn_conv_w"])),
            (conv_b, io["L0_ffn_conv_b"].rearrange("(c p) -> p c", p=P)),
            (dt_b, col(io["L0_ffn_dt_bias"])),
            (a_log, col(io["L0_ffn_A_log"])),
            (norm_w, io["L0_ffn_norm_w"].rearrange("(c p) -> p c", p=P)),
            (w_out, by_tile(io["L0_ffn_W_out"])),
            (w_lin, by_tile(io["L0_ffn_W_lin"])),
            (b_lin, io["L0_ffn_b_lin"].partition_broadcast(P)),
            (w_rel, io["L1_gnn_weight"].rearrange("r (k p) o -> p r k o", p=P)),
            (b_rel, io["L1_gnn_bias"].partition_broadcast(P)),
            (gate_w, by_tile(io["L1_ffn_gate_w"])),
        ]
        gb = io["L1_ffn_gate_b"].partition_broadcast(P)
        small += [(gate_b[:, t, :], gb) for t in range(T)]
        d_pair = io["L0_ffn_D"].rearrange("(j two) -> two j", two=2)
        small += [(d_col[HD * i:HD * (i + 1), :], d_pair[i].partition_broadcast(HD)) for i in range(2)]

        x_v = x_d.rearrange("b (t p) d -> b p t d", p=P)
        adj_v = adj_d.rearrange("b (t p) d -> b p t d", p=P)
        adjt_v = adjt_d.rearrange("b (t p) d -> b p t d", p=P)
        rows_v = rows_d.rearrange("(b t p) d -> b p t d", t=T, p=P)
        x3_v = out[0:NT, :].rearrange("(b t p) d -> b p t d", t=T, p=P)
        ids_v = ids_d[0:SLOTS, :].rearrange("(e p c) o -> e p (c o)", e=E, p=P)
        w1_v = io["L1_ffn_w1"].rearrange("e (k p) f -> e p k f", p=P)
        w2_v = io["L1_ffn_w2"].rearrange("e (k p) f -> e p k f", p=P)
        b1_v = io["L1_ffn_b1"].rearrange("e (c p) -> e p c", p=P)
        EDMA = 4 * 16

        sites = [0]

        def carry(eng):
            sites[0] += 1
            beat = beats[:, sites[0] % BEATS:sites[0] % BEATS + 1]
            if eng is pool_engine[0]:
                return nc.gpsimd.tensor_tensor(beat, mhalf[:, 0:1], mhalf[:, 0:1], ALU.mult)
            else:
                nc.vector.memset(beat, 0.0)

        pool_engine = [None]

        def rounds(eng, step):
            step(0, None, None)
            step(1, 0, None)
            with eng.Fori(2, NB) as k:
                step(k, k - 1, k - 2)
            step(None, NB - 1, NB - 2)
            step(None, None, NB - 1)

        def expert_groups(eng, body):
            with eng.Fori(0, E // 2 - 1) as r:
                for i in range(2):
                    for q in range(EG):
                        body(r, i, q, False)
            for i in range(2):
                for q in range(EG):
                    body(E // 2 - 1, i, q, i == 1 and q == EG - 1)

        def after(r, i, q):
            if q + 1 < EG:
                return r, i, q + 1
            return (r, 1, 0) if i == 0 else (r + 1, 0, 0)

        def count(r, i, q):
            return 2 * EG * r + EG * i + q

        def count_own(r, i, q):
            return EG * r + (EG * i + q) // 2, (EG * i + q) % 2

        block = ctx.enter_context(nc.Block())

        @block.sync
        def _(sp):
            for dst, src in small:
                sp.dma_start(dst[:] if not isinstance(dst, bass.AP) else dst, src).then_inc(loads, 16)

            def step(b1_, b2_, b3_):
                if b1_ is not None:
                    need(sp, x1_ready, b1_)
                    sp.dma_start(x[:], x_v[b1_]).then_inc(x_in, 16)
                    need(sp, noedge_ready, b1_)
                    sp.dma_start(adj[:], adj_v[b1_]).then_inc(adj_in, 16)
                if b3_ is not None:
                    need(sp, masks_ready, b3_)
                    sp.dma_start(adjt[:], adjt_v[b3_]).then_inc(adjt_in, 16)
                    sp.wait_ge(x3_ready, b3_ + 1)
                    sp.dma_start(x3_v[b3_], row[:, :, 0:D]).then_inc(x3_out, 16)
                    sp.wait_ge(row_ready, b3_ + 1)
                    sp.dma_start(rows_v[b3_], row[:]).then_inc(rows_out, 16)

            rounds(sp, step)

            sp.wait_ge(ids_out, 16 * T * NB)
            sp.wait_ge(x3_out, 16 * NB)
            sp.wait_ge(rows_out, 16 * NB)
            with sp.Fori(0, E // 2) as r:
                for i in range(2):
                    sp.wait_ge(expert_done[i], r)
                    sp.dma_start(ids[i][:], ids_v[2 * r + i]).then_inc(eid_in[i], 16)
                    sp.dma_start(w1[i][:], w1_v[2 * r + i]).then_inc(ew_in[i], 16)
                    sp.dma_start(w2[i][:], w2_v[2 * r + i]).then_inc(ew_in[i], 16)
                    sp.dma_start(b1[i][:], b1_v[2 * r + i]).then_inc(ew_in[i], 16)
                    sp.dma_start(b2[i][:], io["L1_ffn_b2"][2 * r + i].partition_broadcast(P)).then_inc(ew_in[i], 16)

        @block.gpsimd
        def _(pool):
            gp = nc.gpsimd
            pool_engine[0] = pool
            gp.memset(ones_row[:], 1.0)
            gp.memset(mhalf[:], -0.5)
            gp.memset(onesb[:], 1.0)
            gp.memset(row[:], 0.0)
            gp.memset(cs3[:], 0.0)
            for a, v in ((cpos, 1e4), (cneg, -1e4), (czero, 0.0)):
                gp.memset(a[:], v)
            gp.memset(negmask[:], 0.0)
            gp.memset(sel[:], 0.0)
            gp.memset(selneg[:], 0.0)
            gp.memset(identb[:], 0.0)
            gp.memset(identf[:], 0.0).then_inc(built, 1)
            pool.wait_ge(built, 1)
            for a in (identf, identb):
                gp.affine_select(a[:], a[:], [[-1, P]], ALU.not_equal, 1.0, base=0, channel_multiplier=1)
            gp.affine_select(triub[:], onesb[:], [[1, P]], ALU.is_ge, 0.0, base=0, channel_multiplier=-1)
            gp.affine_select(negmask[:], negmask[:], [[1, P]], ALU.is_ge, NEG_MASK, base=0, channel_multiplier=-1)
            for i, part in enumerate((0, 32, 64)):
                if i:
                    pool.wait_ge(built, 1 + i)
                gp.affine_select(sel[:], sel[:], [[-1, H], [0, P]], ALU.not_equal, 1.0, base=-part,
                                 channel_multiplier=1)
                gp.affine_select(selneg[:], selneg[:], [[-1, H], [0, N]], ALU.not_equal, -1.0, base=-part,
                                 channel_multiplier=1).then_inc(built, 1)
            gp.iota(base[:], [[CAP, E]], base=0, channel_multiplier=0, allow_small_or_imprecise_dtypes=True)
            gp.iota(lim[:], [[0, T], [CAP, E]], base=CAP, channel_multiplier=0, allow_small_or_imprecise_dtypes=True)
            gp.iota(rev[:], [[0, T], [-1, E]], base=E, channel_multiplier=0, allow_small_or_imprecise_dtypes=True)
            gp.iota(tokf[:], [[P, T]], base=-N, channel_multiplier=1, allow_small_or_imprecise_dtypes=True)
            gp.iota(ids_init[:], [[1, SLOTS // P]], base=NT, channel_multiplier=SLOTS // P).then_inc(built, 1)
            pool.wait_ge(built, 5)
            pool.dma_start(ids_d[0:SLOTS, :].rearrange("(p f) o -> p (f o)", p=P), ids_init[:]).then_inc(ids_set, 16)
            pool.wait_ge(ids_set, 16)

            def rsqrt(i, b):
                pool.wait_ge(var_ready[i], b + 1)
                gp.tensor_tensor(rstd[i][:], ve[i][:], mhalf[:], ALU.pow).then_inc(rstd_ready[i], 1)

            def step(b1_, b2_, b3_):
                if b3_ is not None:
                    rsqrt(2, b3_)
                if b1_ is not None:
                    rsqrt(0, b1_)
                if b2_ is not None:
                    if isinstance(b2_, int) and b2_ == 0:
                        pool.wait_ge(loads, 16 * len(small))
                    pool.wait_ge(x1_ready, b2_ + 1)
                    need(pool, x2_ready, b2_)
                    for t in range(T):
                        last = gp.tensor_tensor(x1b[:, t, :], x1[:, t, :], b_lin[:], ALU.add)
                    last.then_inc(x1b_ready, 1)
                if b3_ is not None:
                    pool.wait_ge(x2_ready, b3_ + 1)
                    need(pool, x3_ready, b3_)
                    pool.wait_ge(adjt_in, 16 * (b3_ + 1))
                    need(pool, h_made, 4 * b3_)
                    if b1_ is not None:
                        pool.wait_ge(adj_in, 16 * (b1_ + 1))
                        need(pool, e_ready, b1_)
                    for t in range(T):
                        last = gp.tensor_tensor(x2b[:, t, :], x2[:, t, :], b_rel[:], ALU.add)
                    last.then_inc(x2b_ready, 1)
                    for r in range(R):
                        last = gp.tensor_scalar(masks[:, :, r, :], adjt[:], float(r + 1), None, ALU.is_equal)
                    last.then_inc(masks_ready, 1)
                if b1_ is not None:
                    if b3_ is None:
                        pool.wait_ge(adj_in, 16 * (b1_ + 1))
                        need(pool, e_ready, b1_)
                    gp.tensor_scalar(noedge[:], adj[:], 0.0, NEG_BIG, ALU.is_le, ALU.mult).then_inc(noedge_ready, 1)
                    rsqrt(1, b1_)
                if b3_ is not None:
                    rsqrt(3, b3_)
                if b2_ is not None:
                    rsqrt(4, b2_)
                if b3_ is not None:
                    pool.wait_ge(slot_ready, b3_ + 1)
                    carry(pool)
                    for t in range(T):
                        gp.indirect_dma_start(
                            ids_d, bass.IndirectOffsetOnAxis(slot[:, t:t + 1], 0), tid[:, t:t + 1], None,
                        ).then_inc(ids_out, 16)

            rounds(pool, step)

            pool.wait_ge(x3_out, 16 * NB)
            pool.wait_ge(rows_out, 16 * NB)

            def gather(r, i, q):
                own, s = count_own(r, i, q)
                if q == 0:
                    pool.wait_ge(idc_ready, 2 * r + i + 1)
                if not (isinstance(r, int) and count(r, i, q) < 2):
                    pool.wait_ge(yo_ready, count(r, i, q) - 1)
                carry(pool).then_inc(carried, 1)
                for j in range(TG):
                    c = q * TG + j
                    gp.indirect_dma_start(
                        xg[s][:, j, :], None, rows_d, bass.IndirectOffsetOnAxis(idc[i][:, c:c + 1], 0),
                    ).then_inc(gath[s], 16)

            def body(r, i, q, last):
                own, s = count_own(r, i, q)
                if not last:
                    gather(*after(r, i, q))
                pool.wait_ge(yo_ready, count(r, i, q) + 1)
                carry(pool).then_inc(carried, 1)
                for j in range(TG):
                    c = q * TG + j
                    gp.indirect_dma_start(
                        out, bass.IndirectOffsetOnAxis(ids[i][:, c:c + 1], 0), yo[s][:, j, :], None,
                    ).then_inc(put[s], 16)
                if q == EG - 1:
                    for k in range(2):
                        own, s = count_own(r, i, q - k)
                        pool.wait_ge(put[s], 16 * TG * (own + 1))
                    pool.sem_inc(expert_done[i], 1)

            gather(0, 0, 0)
            expert_groups(pool, body)
            for s in range(2):
                pool.wait_ge(put[s], 16 * TG * (EG * E // 2))

        @block.scalar
        def _(act):
            def copy(dst, src):
                return nc.scalar.activation(dst, src, ACT.Copy)

            act.wait_ge(loads, 16 * len(small))
            nc.scalar.activation(a_neg[:, 0:1], a_log[:], ACT.Exp).then_inc(prep_a, 1)

            def step(b1_, b2_, b3_):
                if b3_ is not None:
                    act.wait_ge(xn2_ready, b3_ + 1)
                    need(act, h_made, 4 * b3_)
                    copy(xp[0][:], xn2[:]).then_inc(part_a, 1)
                if b2_ is not None:
                    act.wait_ge(proj_made, 5 * b2_ + 1)
                    need(act, dt_ready, b2_)
                    v = bank[2][0:H, N:2 * N]
                    nc.scalar.activation(dt_abs[:], v, ACT.Abs, bias=dt_b[:]).then_inc(dt_act, 1)
                    act.wait_ge(dt_act, 3 * b2_ + 1)
                    nc.scalar.activation(dt_exp[:], dt_abs[:], ACT.Exp, scale=-1.0).then_inc(dt_act, 1)
                    need(act, xs_ready, b2_)
                    for c in (XB, 0, 1, 2, 3):
                        if c in (0, 2):
                            act.wait_ge(proj_made, 5 * b2_ + 2 + c // 2)
                        v = bank[2][:, 0:N] if c == XB else bank[3 + c // 2][:, (c % 2) * N:(c % 2 + 1) * N]
                        ins = nc.scalar.activation(conv[:, c, :], v, ACT.Identity, bias=conv_b[:, c:c + 1],
                                                   scale=conv_w[:, c, TAPS - 1:TAPS])
                        if c in (XB, 1, 3):
                            ins.then_inc(tap_ready, 1)
                    act.wait_ge(dt_act, 3 * b2_ + 2)
                    nc.scalar.activation(dt_ln[:], dt_exp[:], ACT.Ln, bias=1.0).then_inc(dt_act, 1)
                if b1_ is not None:
                    act.wait_ge(xn0_turned, b1_ + 1)
                    need(act, s_made, b1_)
                    copy(xn0T[:], bank[0][:, :]).then_inc(xn0T_ready, 1)
                if b3_ is not None:
                    act.wait_ge(part_v, 2 * b3_ + 1)
                    copy(xp[1][:], xr[:]).then_inc(part_a, 1)
                if b2_ is not None:
                    act.wait_ge(proj_made, 5 * b2_ + 4)
                    need(act, yz_ready, b2_)
                    nc.scalar.activation(zs[:, 0:2, :], bank[5][:, :], ACT.Silu).then_inc(zs_ready, 1)
                    act.wait_ge(proj_made, 5 * b2_ + 5)
                    nc.scalar.activation(zs[:, 2:4, :], bank[2][:, :], ACT.Silu).then_inc(zs_ready, 1)
                    act.wait_ge(conv_ready, 15 * b2_ + 3)
                    need(act, g_made, b2_)
                    nc.scalar.activation(bT[:], conv[0:NS, XB, :], ACT.Silu)
                    nc.scalar.activation(cT[:], conv[NS:P, XB, :], ACT.Silu).then_inc(bc_ready, 1)
                    act.wait_ge(conv_ready, 15 * b2_ + 15)
                    need(act, yd_ready, b2_)
                    nc.scalar.activation(xs[:], conv[:, 0:XB, :], ACT.Silu).then_inc(xs_ready, 1)
                if b1_ is not None:
                    act.wait_ge(wh_made, b1_ + 1)
                    need(act, hp_made, b1_)
                    copy(wh[:], bank[1][:, :]).then_inc(wh_ready, 1)
                    act.wait_ge(s_made, b1_ + 1)
                    copy(s1[:], bank[0][:, N:N + T]).then_inc(s1_ready, 1)
                    act.wait_ge(s1_ready, b1_ + 1)
                    need(act, e_ready, b1_)
                    for t in range(T):
                        ins = nc.scalar.activation(z[:, t, :], bank[0][:, 0:N], ACT.Identity, bias=s1[:, t:t + 1])
                    ins.then_inc(z_ready, 1)
                if b3_ is not None:
                    for c in range(2):
                        act.wait_ge(h_made, 4 * b3_ + c + 1)
                        need(act, gy_made, b3_)
                        copy(hT[:, 0, 512 * c:512 * (c + 1)], bank[6 + c][:, :]).then_inc(hT_ready, 1)
                if b2_ is not None:
                    act.wait_ge(g_made, b2_ + 1)
                    need(act, m_ready, 4 * b2_)
                    copy(g[:], bank[5][:, 0:TRI + T * H]).then_inc(g_ready, 1)
                if b3_ is not None:
                    for c in range(2):
                        act.wait_ge(h_made, 4 * b3_ + c + 3)
                        copy(hT[:, 1, 512 * c:512 * (c + 1)], bank[6 + c][:, :]).then_inc(hT_ready, 1)
                if b1_ is not None:
                    act.wait_ge(e_ready, b1_ + 1)
                    need(act, prob_turned, b1_)
                    for t in range(T):
                        ins = nc.scalar.activation(prob[:, t, :], e[:, t, :], ACT.Exp, bias=nmax[:, t:t + 1],
                                                   accum_out=esum[:, t:t + 1])
                    ins.then_inc(prob_ready, 1)
                for h in range(H):
                    if b2_ is not None:
                        act.wait_ge(expo_made, 8 * b2_ + h + 1)
                        if h == 0:
                            need(act, y_made, 2 * b2_)
                        nc.scalar.activation(decay[:, h, :], bank[EXPO[h % 4]][:, 0:TRI], ACT.Exp).then_inc(decay_ready, 1)
                    if h == 3 and b1_ is not None:
                        act.wait_ge(prob_turned, b1_ + 1)
                        need(act, hp_made, b1_)
                        copy(probT[:], bank[0][:, :]).then_inc(probT_ready, 1)
                if b1_ is not None:
                    act.wait_ge(xn1_turned, b1_ + 1)
                    if b2_ is not None:
                        act.wait_ge(proj_made, 5 * b2_ + 5)
                    copy(xn1T[:], bank[0][:, :]).then_inc(xn1T_ready, 1)
                if b3_ is not None:
                    act.wait_ge(xn3_turned, b3_ + 1)
                    copy(xn3T[:], bank[7][:, :]).then_inc(xn3T_ready, 1)
                if b2_ is not None:
                    act.wait_ge(yz_ready, b2_ + 1)
                    need(act, out_made, b2_)
                    nc.scalar.activation(y2[:], y[:], ACT.Square).then_inc(y2_ready, 1)
                if b3_ is not None:
                    act.wait_ge(lg_ready, b3_ + 1)
                    nc.scalar.activation(ge[:], lg2[:], ACT.Exp).then_inc(ge_ready, 1)

            rounds(act, step)

            def turn(r, i, q):
                for k in range(DK):
                    act.wait_ge(xg_turned, 2 * count(r, i, q) + k + 1)
                    ins = copy(xgT[:, k, :], bank[6 + k][:, :])
                ins.then_inc(xgT_ready, 1)

            def body(r, i, q, last):
                n = count(r, i, q)
                if q == 0:
                    act.wait_ge(ew_in[i], EDMA * (r + 1))
                for f in range(0, FB, 2):
                    act.wait_ge(up_made, FB * n + f + 1)
                    if f == 0:
                        need(act, down_made, n * 2) if not (isinstance(r, int) and n == 0) else None
                    nc.scalar.activation(hid(f), bank[f % 4][:, :], ACT.Relu, bias=b1[i][:, f:f + 1]).then_inc(hid_act, 1)
                if not last:
                    turn(*after(r, i, q))

            turn(0, 0, 0)
            expert_groups(act, body)

        @block.vector
        def _(dve):
            v = nc.vector
            dve.wait_ge(loads, 16 * len(small))
            dve.wait_ge(built, 5)
            for i in range(2):
                for k in range(DK):
                    ins = v.tensor_tensor_reduce(junk[:, i, k, :], w_gat[:, k, :], a_bc[:, i, :], 1.0, 0.0, ALU.mult,
                                                 ALU.add, wa[:, i, k:k + 1])
            ins.then_inc(built_v, 1)
            for c in range(XB):
                ins = v.tensor_scalar(w_out[:, c, :], w_out[:, c, :], norm_w[:, c:c + 1], None, ALU.mult)
            ins.then_inc(prep_v, 1)
            dve.wait_ge(built_v, 1)
            for k in range(DK):
                v.tensor_scalar(wa2[:, k, :], ones_row[:, 0:P], wa[:, 1, k:k + 1], None, ALU.mult)
            dve.wait_ge(prep_a, 1)
            v.tensor_scalar(a_neg[:, 1:2], a_neg[:, 0:1], -1.0, None, ALU.mult).then_inc(prep_v, 1)
            dve.wait_ge(prep_pe, 1)
            for k in range(DK):
                ins = v.tensor_copy(w_outT[:, k, :], bank[k][:, :])
            ins.then_inc(prep_v, 1)
            dve.wait_ge(prep_pe, 2)
            for k in range(2):
                ins = v.tensor_copy(w_proj[:, 2 * k:2 * k + 2, :], bank[2 + k][:, :])
            ins.then_inc(prep_v, 1)
            dve.wait_ge(prep_v, 4)

            def deviation(i, src, chain, b):
                for t in range(T):
                    ins = v.bn_stats(stats[i][:, t, :], src[:, t, :])
                chain.link(dve, ins, b, carry)
                for t in range(T):
                    ins = v.bn_aggr(mv[i][:, t, :], stats[i][:, t, :])
                chain.link(dve, ins, b)
                v.tensor_scalar(ve[i][:], mv[i][:, :, 1], EPS, None, ALU.add).then_inc(var_ready[i], 1)

            def normalise(i, dst, src, done, b):
                dve.wait_ge(rstd_ready[i], b + 1)
                for t in range(T):
                    ins = v.tensor_scalar(dst[:, t, :], src[:, t, :], mv[i][:, t, 0:1], rstd[i][:, t:t + 1],
                                          ALU.subtract, ALU.mult)
                ins.then_inc(done, 1)

            def taps(c, b):
                src = bank[2][:, 0:N] if c == XB else bank[3 + c // 2][:, (c % 2) * N:(c % 2 + 1) * N]
                first = {XB: 0, 0: 3, 1: 6, 2: 9, 3: 12}[c]
                for k in range(1, TAPS):
                    v.scalar_tensor_tensor(conv[:, c, k:N], src[:, 0:N - k], conv_w[:, c, TAPS - 1 - k:TAPS - k],
                                           conv[:, c, k:N], ALU.mult, ALU.add).then_inc(conv_ready, 1)
                    dve.wait_ge(conv_ready, 15 * b + first + k)

            def step(b1_, b2_, b3_):
                for chain in (ch1, ch1b, ch2, ch3, chr_):
                    chain.start()
                if b3_ is not None:
                    deviation(2, x2, ch3, b3_)
                if b1_ is not None:
                    dve.wait_ge(x_in, 16 * (b1_ + 1))
                    deviation(0, x, ch1, b1_)
                if b3_ is not None:
                    normalise(2, xn2, x2, xn2_ready, b3_)
                if b1_ is not None:
                    need(dve, xn0_turned, b1_)
                    normalise(0, xn0, x, xn0_ready, b1_)
                if b2_ is not None:
                    dve.wait_ge(tap_ready, 3 * b2_ + 1)
                    v.tensor_scalar(dt_pos[:], bank[2][0:H, N:2 * N], dt_b[:], 0.0, ALU.add, ALU.max)
                    taps(XB, b2_)
                if b3_ is not None:
                    dve.wait_ge(part_a, 2 * b3_ + 1)
                    v.tensor_tensor(xr[:], xn2[:], xp[0][:], ALU.subtract).then_inc(part_v, 1)
                if b2_ is not None:
                    for c in range(XB):
                        if c % 2 == 0:
                            dve.wait_ge(tap_ready, 3 * b2_ + 2 + c // 2)
                        taps(c, b2_)
                        if c == 0 and b3_ is not None:
                            dve.wait_ge(part_a, 2 * b3_ + 2)
                            v.tensor_tensor(xp[2][:], xr[:], xp[1][:], ALU.subtract).then_inc(part_v, 1)
                    dve.wait_ge(dt_act, 3 * b2_ + 3)
                    need(dve, g_made, b2_)
                    ins = v.tensor_tensor(dt[:], dt_pos[:], dt_ln[:], ALU.add)
                    ins.then_inc(dt_ready, 1)
                    dve.wait_ge(dt_ready, b2_ + 1)
                    ch2.link(dve, v.tensor_scalar(dA[:], dt[:], a_neg[:, 1:2], None, ALU.mult), b2_)
                    ch2.link(dve, v.tensor_tensor_scan(cs[:], ones_row[0:H, :], dA[:], 0.0, ALU.mult, ALU.add), b2_)
                    need(dve, expo_made, 8 * b2_)
                    ch2.link(dve, v.tensor_copy(cs3[0:H, :], cs[:]), b2_)
                    ch2.link(dve, v.tensor_tensor(cs_r[:], cs[:], cs3[0:H, :], ALU.subtract), b2_)
                    v.tensor_copy(cs3[32:32 + H, :], cs_r[:])
                    ch2.link(dve, v.tensor_copy(cs_m[:], cs_r[:]), b2_)
                    v.tensor_tensor(cs3[64:64 + H, :], cs_r[:], cs_m[:], ALU.subtract).then_inc(cs_ready, 1)
                elif b3_ is not None:
                    dve.wait_ge(part_a, 2 * b3_ + 2)
                    v.tensor_tensor(xp[2][:], xr[:], xp[1][:], ALU.subtract).then_inc(part_v, 1)
                if b1_ is not None:
                    dve.wait_ge(z_ready, b1_ + 1)
                    for t in range(T):
                        ins = v.scalar_tensor_tensor(z[:, t, :], z[:, t, :], SLOPE, z[:, t, :], ALU.mult, ALU.max)
                    ch1.link(dve, ins, b1_, carry)
                    dve.wait_ge(noedge_ready, b1_ + 1)
                    carry(dve)
                    for t in range(T):
                        ins = v.tensor_tensor_reduce(e[:, t, :], z[:, t, :], noedge[:, t, :], 1.0, -3e38, ALU.add,
                                                     ALU.max, emax[:, t:t + 1])
                    ch1.link(dve, ins, b1_)
                    v.tensor_scalar(nmax[:], emax[:], -1.0, None, ALU.mult).then_inc(e_ready, 1)
                if b2_ is not None:
                    dve.wait_ge(g_ready, b2_ + 1)
                    need(dve, y_made, 2 * b2_)
                    for t in range(T):
                        dve.wait_ge(x_turned, 2 * b2_ + t + 1)
                        ins = v.tensor_tensor(xdt[:, t, :].rearrange("p (h c) -> p h c", h=H),
                                              bank[3 + t][:, :].rearrange("p (h c) -> p h c", h=H),
                                              dtT[:, t, :].unsqueeze(2).broadcast_to([P, H, HD]), ALU.mult)
                        ins.then_inc(xdt_ready, 1)
                    for j in range(H // 2):
                        dve.wait_ge(decay_ready, 8 * b2_ + 2 * j + 2)
                        v.tensor_tensor(decay[:, 2 * j:2 * j + 2, :], decay[:, 2 * j:2 * j + 2, :],
                                        g[:, 0:TRI].unsqueeze(1).broadcast_to([P, 2, TRI]), ALU.mult).then_inc(m_ready, 1)
                if b1_ is not None:
                    dve.wait_ge(prob_ready, b1_ + 1)
                    ch1.link(dve, v.reciprocal(rsum[:], esum[:]), b1_)
                    dve.wait_ge(hp_made, b1_ + 1)
                    if b2_ is not None:
                        dve.wait_ge(x1b_ready, b2_ + 1)
                    for t in range(T):
                        ins = v.scalar_tensor_tensor(x1[:, t, :], bank[1][:, t * D:(t + 1) * D], rsum[:, t:t + 1],
                                                     x[:, t, :], ALU.mult, ALU.add)
                    ins.then_inc(x1_ready, 1)
                    dve.wait_ge(x1_ready, b1_ + 1)
                    deviation(1, x1, ch1b, b1_)
                if b3_ is not None:
                    dve.wait_ge(gy_made, b3_ + 1)
                    dve.wait_ge(x2b_ready, b3_ + 1)
                    need(dve, x3_out, 16 * b3_)
                    need(dve, rows_out, 16 * b3_)
                    ins = v.tensor_tensor(row[:, :, 0:D], bank[6][:, :].rearrange("p (t d) -> p t d", t=T), x2b[:],
                                          ALU.add)
                    ins.then_inc(x3_ready, 1)
                    dve.wait_ge(x3_ready, b3_ + 1)
                    deviation(3, row[:, :, 0:D], chr_, b3_)
                if b1_ is not None:
                    need(dve, xn1_turned, b1_)
                    normalise(1, xn1, x1, xn1_ready, b1_)
                if b3_ is not None:
                    need(dve, xn3_turned, b3_)
                    normalise(3, xn3, row[:, :, 0:D], xn3_ready, b3_)
                if b2_ is not None:
                    for j in range(XB):
                        if j % 2 == 0:
                            dve.wait_ge(y_made, 2 * b2_ + 1 + j // 2)
                        if j == 0:
                            need(dve, out_made, b2_)
                        ins = v.scalar_tensor_tensor(y[:, j, :], xs[:, j, :], d_col[:, j:j + 1],
                                                     bank[2 + j // 2][:, (j % 2) * N:(j % 2 + 1) * N], ALU.mult, ALU.add)
                    ins.then_inc(yd_ready, 1)
                    dve.wait_ge(yd_ready, b2_ + 1)
                    v.tensor_tensor(y[:], y[:], zs[:], ALU.mult).then_inc(yz_ready, 1)
                if b3_ is not None:
                    dve.wait_ge(gate_made, b3_ + 1)
                    lk = lambda ins: chr_.link(dve, ins, b3_)
                    three = lambda a: a.unsqueeze(2).broadcast_to([P, T, E])
                    lk(v.tensor_tensor(lg[:], bank[6][:, 0:T * E].rearrange("p (t e) -> p t e", t=T), gate_b[:], ALU.add))
                    lk(v.tensor_reduce(lmax[:], lg[:], AX.X, ALU.max))
                    v.tensor_tensor(lg2[:], lg[:], three(lmax[:]), ALU.subtract).then_inc(lg_ready, 1)
                    dve.wait_ge(ge_ready, b3_ + 1)
                    v.tensor_reduce(gsum[:], ge[:], AX.X, ALU.add)
                    lk(v.tensor_reduce(gmax[:], ge[:], AX.X, ALU.max))
                    v.reciprocal(grec[:], gsum[:])
                    lk(v.tensor_tensor(eq[:], ge[:], three(gmax[:]), ALU.is_equal))
                    v.tensor_tensor(prb[:], gmax[:], grec[:], ALU.mult)
                    lk(v.tensor_tensor(rv[:], eq[:], rev[:], ALU.mult))
                    lk(v.tensor_reduce(rmax[:], rv[:], AX.X, ALU.max))
                    need(dve, cum_made, b3_)
                    v.tensor_tensor(ohb[:], rev[:], three(rmax[:]), ALU.is_equal).then_inc(oh_ready, 1)
                    v.tensor_tensor(oh[:], rev[:], three(rmax[:]), ALU.is_equal)
                    need(dve, ids_out, 16 * T * b3_)
                    lk(v.tensor_scalar(tokf[:], tokf[:], float(N), None, ALU.add))
                    v.tensor_copy(tid[:], tokf[:])
                    v.tensor_scalar(tr1[:], tokf[:], float(SLOTS + 1), None, ALU.add)
                    dve.wait_ge(cum_made, b3_ + 1)
                    v.tensor_tensor(limo[:], lim[:], oh[:], ALU.mult)
                    lk(v.tensor_tensor(cum[:], bank[7][:, 0:T * E].rearrange("p (t e) -> p t e", t=T),
                                       base[:].unsqueeze(1).broadcast_to([P, T, E]), ALU.add))
                    v.tensor_tensor(base[:], base[:], bank[7][:, T * E:T * E + E], ALU.add).then_inc(base_ready, 1)
                    lk(v.tensor_tensor(cumo[:], cum[:], oh[:], ALU.mult))
                    v.tensor_reduce(lm[:], limo[:], AX.X, ALU.add)
                    lk(v.tensor_reduce(slot1[:], cumo[:], AX.X, ALU.add))
                    v.tensor_tensor(kept[:], slot1[:], lm[:], ALU.is_le)
                    lk(v.tensor_tensor(df[:], slot1[:], tr1[:], ALU.subtract))
                    lk(v.tensor_tensor(kd[:], kept[:], df[:], ALU.mult))
                    lk(v.scalar_tensor_tensor(df[:], kd[:], -1.0, tr1[:], ALU.add, ALU.add))
                    v.tensor_copy(slot[:], df[:]).then_inc(slot_ready, 1)
                    v.tensor_copy(row[:, :, D:D + 1], mv[3][:, :, 0:1])
                    v.tensor_copy(row[:, :, D + 1], rstd[3][:])
                    v.tensor_tensor(row[:, :, D + 2], prb[:], kept[:], ALU.mult).then_inc(row_ready, 1)
                if b2_ is not None:
                    dve.wait_ge(out_made, b2_ + 1)
                    v.tensor_scalar(ve[4][:], bank[5][:, 0:T], 1.0 / DIN, EPS, ALU.mult, ALU.add).then_inc(var_ready[4], 1)
                    dve.wait_ge(rstd_ready[4], b2_ + 1)
                    dve.wait_ge(x1b_ready, b2_ + 1)
                    if b3_ is not None:
                        dve.wait_ge(x2b_ready, b3_ + 1)
                    for t in range(T):
                        ins = v.scalar_tensor_tensor(x2[:, t, :], bank[4][:, t * D:(t + 1) * D], rstd[4][:, t:t + 1],
                                                     x1b[:, t, :], ALU.mult, ALU.add)
                    ins.then_inc(x2_ready, 1)
                    dve.wait_ge(x2_ready, b2_ + 1)

            rounds(dve, step)

            def normalise_group(r, i, q):
                own, s = count_own(r, i, q)
                if q == 0:
                    dve.wait_ge(eid_in[i], 16 * (r + 1))
                dve.wait_ge(gath[s], 16 * TG * (own + 1))
                if not (isinstance(r, int) and count(r, i, q) == 0):
                    dve.wait_ge(xg_turned, 2 * count(r, i, q))
                for j in range(TG):
                    ins = v.tensor_scalar(xgn[:, j, :], xg[s][:, j, 0:D], xg[s][:, j, D:D + 1], xg[s][:, j, D + 1:D + 2],
                                          ALU.subtract, ALU.mult)
                ins.then_inc(xgn_ready, 1)

            def clamp_ids(r, i):
                dve.wait_ge(eid_in[i], 16 * (r + 1))
                v.tensor_scalar(idc[i][:], ids[i][:], float(NT - 1), None, ALU.min).then_inc(idc_ready, 1)

            def body(r, i, q, last):
                n = count(r, i, q)
                own, s = count_own(r, i, q)
                for f in range(1, FB, 2):
                    dve.wait_ge(up_made, FB * n + f + 1)
                    if f == 1 and not (isinstance(r, int) and n == 0):
                        dve.wait_ge(down_made, 2 * n)
                    v.tensor_scalar(hid(f), bank[f % 4][:, :], b1[i][:, f:f + 1], 0.0, ALU.add, ALU.max).then_inc(hid_dve, 1)
                    if f == 1:
                        if q == 2 and not (last_round(r) and i == 1):
                            clamp_ids(r + i, 1 - i)
                        if not last:
                            normalise_group(*after(r, i, q))
                if not (isinstance(r, int) and n < 2):
                    dve.wait_ge(put[s], 16 * TG * own)
                dve.wait_ge(carried, 2 * n + 1)
                for u in range(2):
                    dve.wait_ge(down_made, 2 * n + u + 1)
                    ins = v.tensor_tensor(yo[s][:, 2 * u:2 * u + 2, :],
                                          bank[4 + u][:, :].rearrange("p (j d) -> p j d", j=2),
                                          b2[i][:].unsqueeze(1).broadcast_to([P, 2, D]), ALU.add)
                ins.then_inc(sum_ready, 1)
                dve.wait_ge(sum_ready, n + 1)
                lk = lambda ins: che.link(dve, ins, n)
                che.start()
                for j in range(TG):
                    ins = v.tensor_scalar(yo[s][:, j, :], yo[s][:, j, :], xg[s][:, j, D + 2:D + 3], None, ALU.mult)
                lk(ins)
                v.tensor_scalar(isp, yo[s][:], float("inf"), None, ALU.is_equal)
                v.tensor_scalar(isn, yo[s][:], float("-inf"), None, ALU.is_equal)
                che.link(dve, v.tensor_tensor(isnan, yo[s][:], yo[s][:], ALU.not_equal), n, carry)
                for mask, value in ((isp, cpos), (isn, cneg), (isnan, czero)):
                    che.link(dve, v.copy_predicated(yo[s][:], mask, value[:].unsqueeze(1).broadcast_to([P, TG, D])),
                             n, carry)
                v.tensor_tensor(yo[s][:], yo[s][:], xg[s][:, :, 0:D], ALU.add).then_inc(yo_ready, 1)

            def last_round(r):
                return isinstance(r, int) and r == E // 2 - 1

            clamp_ids(0, 0)
            normalise_group(0, 0, 0)
            expert_groups(dve, body)

        @block.tensor
        def _(pe):
            mm, turn = nc.tensor.matmul, nc.tensor.transpose

            pe.wait_ge(built, 5)
            pe.wait_ge(prep_v, 1)
            for k in range(DK):
                for c in range(XB):
                    ins = turn(bank[k][:, c * P:(c + 1) * P], w_out[:, c, k * P:(k + 1) * P], identf[:])
            ins.then_inc(prep_pe, 1)
            pe.wait_ge(prep_v, 3)
            for c in range(XB):
                for k in range(DK):
                    ins = mm(bank[2 + c // 2][:, (c % 2) * D:(c % 2 + 1) * D], w_outT[:, k, c * P:(c + 1) * P],
                             w_lin[:, k, :], start=k == 0, stop=k == DK - 1)
            ins.then_inc(prep_pe, 1)
            pe.wait_ge(prep_v, 4)

            def turn_pair(dst, src):
                for k in range(DK):
                    for t in range(T):
                        ins = turn(dst[:, k * N + t * P:k * N + (t + 1) * P], src[:, t, k * P:(k + 1) * P], identf[:])
                return ins

            def project(dst, first, width=P):
                for k in range(DK):
                    ins = mm(dst, w_in[:, k, first:first + width], xn1T[:, k, :], start=k == 0, stop=k == DK - 1)
                return ins

            def step(b1_, b2_, b3_):
                if b2_ is not None:
                    pe.wait_ge(xn1T_ready, b2_ + 1)
                    need(pe, yd_ready, b2_)
                    project(bank[2][:, 0:N], DIN + DIN)
                    project(bank[2][0:H, N:2 * N], 2 * DIN + 2 * NS, H).then_inc(proj_made, 1)
                    for u in range(2):
                        if u == 1:
                            need(pe, x2_ready, b2_)
                        for c in (2 * u, 2 * u + 1):
                            ins = project(bank[3 + u][:, (c % 2) * N:(c % 2 + 1) * N], DIN + c * P)
                        ins.then_inc(proj_made, 1)
                    for c in range(2):
                        ins = project(bank[5][:, c * N:(c + 1) * N], c * P)
                    ins.then_inc(proj_made, 1)
                if b1_ is not None:
                    pe.wait_ge(xn0_ready, b1_ + 1)
                    need(pe, xn1T_ready, b1_)
                    turn_pair(bank[0], xn0).then_inc(xn0_turned, 1)
                if b2_ is not None:
                    pe.wait_ge(conv_ready, 15 * b2_ + 3)
                    pe.wait_ge(dt_act, 3 * b2_ + 1)
                    for c in range(2, 4):
                        ins = project(bank[2][:, (c % 2) * N:(c % 2 + 1) * N], c * P)
                    ins.then_inc(proj_made, 1)
                if b1_ is not None:
                    pe.wait_ge(xn0T_ready, b1_ + 1)
                    need(pe, x1_ready, b1_)
                    for t in range(T):
                        for k in range(DK):
                            ins = mm(bank[1][:, t * D:(t + 1) * D], xn0T[:, k, t * P:(t + 1) * P], w_gat[:, k, :],
                                     start=k == 0, stop=k == DK - 1)
                    ins.then_inc(wh_made, 1)
                    for k in range(DK):
                        mm(bank[0][:, 0:N], wa2[:, k, :], xn0T[:, k, :], start=k == 0, stop=k == DK - 1)
                    for t in range(T):
                        for k in range(DK):
                            ins = mm(bank[0][:, N + t:N + t + 1], xn0T[:, k, t * P:(t + 1) * P], wa[:, 0, k:k + 1],
                                     start=k == 0, stop=k == DK - 1)
                    ins.then_inc(s_made, 1)
                if b3_ is not None:
                    pe.wait_ge(part_v, 2 * b3_ + 2)
                    pe.wait_ge(masks_ready, b3_ + 1)
                    for d in range(DK):
                        for c in range(2):
                            if d == 0:
                                need(pe, base_ready, b3_)
                            else:
                                pe.wait_ge(hT_ready, 4 * b3_ + c + 1)
                            for t in range(T):
                                for part in range(3):
                                    ins = mm(bank[6 + c][:, :], xp[part][:, t, d * P:(d + 1) * P],
                                             masks[:, t, 2 * c:2 * c + 2, :], start=t == 0 and part == 0,
                                             stop=t == T - 1 and part == 2)
                            ins.then_inc(h_made, 1)
                if b2_ is not None:
                    pe.wait_ge(dt_ready, b2_ + 1)
                    pe.wait_ge(zs_ready, 2 * b2_ + 1)
                    pe.wait_ge(bc_ready, b2_ + 1)
                    mm(bank[5][:, 0:N], bT[:, 0:P], cT[:], start=True, stop=True)
                    mm(bank[5][:, N:TRI], bT[:, P:N], cT[:, P:N], start=True, stop=True)
                    for t in range(T):
                        ins = turn(bank[5][:, TRI + t * H:TRI + (t + 1) * H], dt[:, t * P:(t + 1) * P],
                                   identf[0:H, 0:H])
                    ins.then_inc(g_made, 1)
                    pe.wait_ge(xs_ready, b2_ + 1)
                    for t in range(T):
                        for c in range(XB):
                            ins = turn(bank[3 + t][:, c * P:(c + 1) * P], xs[:, c, t * P:(t + 1) * P], identf[:])
                        ins.then_inc(x_turned, 1)
                if b1_ is not None:
                    pe.wait_ge(prob_ready, b1_ + 1)
                    for k in range(T):
                        for t in range(T):
                            ins = turn(bank[0][:, k * N + t * P:k * N + (t + 1) * P], prob[:, t, k * P:(k + 1) * P],
                                       identf[:])
                    ins.then_inc(prob_turned, 1)
                if b2_ is not None:
                    pe.wait_ge(cs_ready, b2_ + 1)
                    for h in range(H):
                        if h == 0:
                            pe.wait_ge(zs_ready, 2 * b2_ + 2)
                        elif h == 1:
                            pe.wait_ge(g_ready, b2_ + 1)
                        elif h in (2, 3):
                            pe.wait_ge(xdt_ready, 2 * b2_ + h - 1)
                        else:
                            pe.wait_ge(decay_ready, 8 * b2_ + h - 3)
                        o = bank[EXPO[h % 4]]
                        for first, width, s, l in ((0, N, 0, 0), (N, TRI - N, P, P)):
                            mm(o[:, first:first + width], sel[:, h, :], cs3[:, l:N], start=True, stop=False)
                            mm(o[:, first:first + P], identb[:], negmask[:], start=False, stop=False,
                               skip_group_check=True)
                            ins = mm(o[:, first:first + width], cs3[:, s:s + P], selneg[:, h, 0:width], start=False,
                                     stop=True)
                        ins.then_inc(expo_made, 1)
                if b1_ is not None:
                    pe.wait_ge(probT_ready, b1_ + 1)
                    pe.wait_ge(wh_ready, b1_ + 1)
                    for t in range(T):
                        for k in range(T):
                            ins = mm(bank[1][:, t * D:(t + 1) * D], probT[:, k, t * P:(t + 1) * P], wh[:, k, :],
                                     start=k == 0, stop=k == T - 1)
                    ins.then_inc(hp_made, 1)
                if b3_ is not None:
                    pe.wait_ge(hT_ready, 4 * b3_ + 4)
                    for t in range(T):
                        for r in range(R):
                            for d in range(DK):
                                ins = mm(bank[6][:, t * D:(t + 1) * D], hT[:, d, r * N + t * P:r * N + (t + 1) * P],
                                         w_rel[:, r, d, :], start=r == 0 and d == 0, stop=r == R - 1 and d == DK - 1)
                    ins.then_inc(gy_made, 1)
                if b2_ is not None:
                    pe.wait_ge(decay_ready, 8 * b2_ + 8)
                    for h in range(H):
                        if h % 2 == 0:
                            pe.wait_ge(m_ready, 4 * b2_ + h // 2 + 1)
                        j = h // 2
                        o = bank[2 + j // 2][HD * (h % 2):HD * (h % 2 + 1), (j % 2) * N:(j % 2 + 1) * N]
                        mm(o, xdt[:, 0, h * HD:(h + 1) * HD], decay[:, h, 0:N], start=True, stop=True)
                        ins = mm(o[:, P:N], xdt[:, 1, h * HD:(h + 1) * HD], decay[:, h, N:TRI], start=False, stop=True,
                                 skip_group_check=True)
                        if h % 4 == 3:
                            ins.then_inc(y_made, 1)
                if b1_ is not None:
                    pe.wait_ge(xn1_ready, b1_ + 1)
                    turn_pair(bank[0], xn1).then_inc(xn1_turned, 1)
                if b3_ is not None:
                    pe.wait_ge(xn3_ready, b3_ + 1)
                    turn_pair(bank[7], xn3).then_inc(xn3_turned, 1)
                    pe.wait_ge(xn3T_ready, b3_ + 1)
                    for t in range(T):
                        for k in range(DK):
                            ins = mm(bank[6][:, t * E:(t + 1) * E], xn3T[:, k, t * P:(t + 1) * P], gate_w[:, k, :],
                                     start=k == 0, stop=k == DK - 1)
                    ins.then_inc(gate_made, 1)
                if b2_ is not None:
                    pe.wait_ge(y2_ready, b2_ + 1)
                    for t in range(T):
                        for j in range(XB):
                            mm(bank[5][:, t:t + 1], y2[:, j, t * P:(t + 1) * P], ones_row[:, 0:1],
                               start=j == 0, stop=j == XB - 1)
                    for t in range(T):
                        for j in range(XB):
                            ins = mm(bank[4][:, t * D:(t + 1) * D], y[:, j, t * P:(t + 1) * P], w_proj[:, j, :],
                                     start=j == 0, stop=j == XB - 1)
                    ins.then_inc(out_made, 1)
                if b3_ is not None:
                    pe.wait_ge(oh_ready, b3_ + 1)
                    mm(bank[7][:, 0:E], triub[:], ohb[:, 0, :], start=True, stop=True)
                    for first in (E, 2 * E):
                        mm(bank[7][:, first:first + E], onesb[:], ohb[:, 0, :], start=True, stop=False)
                        ins = mm(bank[7][:, first:first + E], triub[:] if first == E else onesb[:], ohb[:, 1, :],
                                 start=False, stop=True)
                    ins.then_inc(cum_made, 1)

            rounds(pe, step)

            def turn_group(r, i, q):
                n = count(r, i, q)
                pe.wait_ge(xgn_ready, n + 1)
                if not (isinstance(r, int) and n == 0):
                    pe.wait_ge(xgT_ready, n)
                for k in range(DK):
                    for j in range(TG):
                        ins = turn(bank[6 + k][:, j * P:(j + 1) * P], xgn[:, j, k * P:(k + 1) * P], identf[:])
                    ins.then_inc(xg_turned, 1)

            def body(r, i, q, last):
                n = count(r, i, q)
                if q == 0:
                    pe.wait_ge(ew_in[i], EDMA * (r + 1))
                pe.wait_ge(xgT_ready, n + 1)
                for f in range(FB):
                    if f >= 4:
                        pe.wait_ge((hid_act, hid_dve)[f % 2], 4 * n + (f - 4) // 2 + 1)
                    for k in range(DK):
                        ins = mm(bank[f % 4][:, :], w1[i][:, k, f * P:(f + 1) * P], xgT[:, k, :], start=k == 0,
                                 stop=k == DK - 1)
                    ins.then_inc(up_made, 1)
                if not last:
                    turn_group(*after(r, i, q))
                pe.wait_ge(hid_act, 4 * n + 4)
                pe.wait_ge(hid_dve, 4 * n + 4)
                if not (isinstance(r, int) and n == 0):
                    pe.wait_ge(sum_ready, n)
                for j in range(TG):
                    for f in range(FB):
                        ins = mm(bank[4 + j // 2][:, (j % 2) * D:(j % 2 + 1) * D], hid(f)[:, j * P:(j + 1) * P],
                                 w2[i][:, f, :], start=f == 0, stop=f == FB - 1)
                    if j % 2:
                        ins.then_inc(down_made, 1)

            turn_group(0, 0, 0)
            expert_groups(pe, body)


INPUTS = ['x', 'adj', 'L0_gnn_W', 'L0_gnn_a', 'L0_ffn_W_in', 'L0_ffn_conv_w', 'L0_ffn_conv_b', 'L0_ffn_dt_bias',
          'L0_ffn_A_log', 'L0_ffn_D', 'L0_ffn_norm_w', 'L0_ffn_W_out', 'L0_ffn_W_lin', 'L0_ffn_b_lin',
          'L1_gnn_weight', 'L1_gnn_bias', 'L1_ffn_gate_w', 'L1_ffn_gate_b', 'L1_ffn_w1', 'L1_ffn_b1', 'L1_ffn_w2',
          'L1_ffn_b2']


def kernel(**inputs):
    import numpy as np
    import concourse.bacc as bacc
    from concourse.bass_utils import run_bass_kernel_spmd

    nc = bacc.Bacc("TRN2", target_bir_lowering=False, num_devices=1)
    arrays, io = {}, {}
    given = {name: np.ascontiguousarray(inputs[name]) for name in INPUTS}
    given["adjT"] = np.ascontiguousarray(given["adj"].transpose(0, 2, 1))
    for name, a in given.items():
        arrays[f"in_{name}"] = a
        io[name] = nc.dram_tensor(f"in_{name}", a.shape, mybir.dt.from_np(a.dtype), kind="ExternalInput").ap()
    nb, n, d = given["x"].shape
    experts = given["L1_ffn_gate_w"].shape[1]
    tokens = nb * n
    slots = experts * -(-5 * tokens // (4 * experts))
    out = nc.dram_tensor("out", (tokens + slots, d), F32, kind="ExternalOutput").ap()
    graph_mamba_moe(nc, io, out)
    got = run_bass_kernel_spmd(nc, [arrays], core_ids=[0]).results[0]["out"]
    return np.asarray(got)[0:tokens].reshape(nb, n, d)
```
